# Optimizing a Trainium2 kernel written in Bass

```python
import numpy as np
import jax
import jax.numpy as jnp

def _softmax(x, axis=-1):
    return jax.nn.softmax(x, axis=axis)

def _gelu(x):
    return jax.nn.gelu(x, approximate=True)

def _silu(x):
    return jax.nn.silu(x)

def _sigmoid(x):
    return jax.nn.sigmoid(x)

def _layernorm(x, axis=-1, eps=1e-05):
    m = jnp.mean(x, axis=axis, keepdims=True)
    v = jnp.var(x, axis=axis, keepdims=True)
    return (x - m) / jnp.sqrt(v + eps)

def _scatter_add(tgt, idx, src, axis=0):
    return tgt.at[idx].add(src)

def _segment_sum(src, seg, n):
    return jax.ops.segment_sum(src, seg, n)
kernel_name = 'mk_prb_d1_jaxref_r8_250adb'

def setup_inputs(seed: int=0):
    np.random.seed(seed)
    _w = jnp.asarray

    def _L0_attn_setup():
        import jax, jax.numpy as jnp
        import numpy as np
        D_MODEL = 128
        D_STATE = 16
        D_CONV = 4
        EXPAND = 2
        D_INNER = EXPAND * D_MODEL
        DT_RANK = (D_MODEL + 15) // 16
        BATCH = 2
        SEQLEN = 128

        def _causal_conv_silu(x, w, b):
            k = w.shape[-1]
            y = jax.lax.conv_general_dilated(x, w, window_strides=(1,), padding=[(k - 1, 0)], dimension_numbers=('NCH', 'OIH', 'NCH'), feature_group_count=x.shape[1])
            return jax.nn.silu(y + b[None, :, None])

        def _ssm_scan(dA, dBx):

            def op(e1, e2):
                a1, b1 = e1
                a2, b2 = e2
                return (a1 * a2, a2 * b1 + b2)
            return jax.lax.associative_scan(op, (dA, dBx), axis=2)[1]

        def _mamba_dir(xz, conv_w, conv_b, xproj_w, dtproj_w, dt_bias, A_log, Dp):
            d_inner = xz.shape[1] // 2
            x, z = (xz[:, :d_inner], xz[:, d_inner:])
            u = _causal_conv_silu(x, conv_w, conv_b)
            x_dbl = jnp.einsum('bdl,kd->bkl', u, xproj_w)
            n = A_log.shape[1]
            r = dtproj_w.shape[1]
            delta = jnp.einsum('dr,brl->bdl', dtproj_w, x_dbl[:, :r])
            Bm = x_dbl[:, r:r + n]
            Cm = x_dbl[:, r + n:]
            delta = jax.nn.softplus(delta + dt_bias[None, :, None])
            A = -jnp.exp(A_log)
            dA = jnp.exp(jnp.einsum('bdl,dn->bdln', delta, A))
            dBx = jnp.einsum('bdl,bnl,bdl->bdln', delta, Bm, u)
            h = _ssm_scan(dA, dBx)
            y = jnp.einsum('bdln,bnl->bdl', h, Cm)
            y = y + Dp[None, :, None] * u
            return y * jax.nn.silu(z)
        key = jax.random.key(seed)
        ks = jax.random.split(key, 16)
        s_in = 1.0 / np.sqrt(D_MODEL)
        s_x = 1.0 / np.sqrt(D_INNER)
        dt_std = DT_RANK ** (-0.5)

        def dt_bias_init(k):
            dt = jnp.exp(jax.random.uniform(k, (D_INNER,)) * (np.log(0.1) - np.log(0.001)) + np.log(0.001))
            dt = jnp.clip(dt, 0.0001, None)
            return dt + jnp.log(-jnp.expm1(-dt))
        A_log = jnp.log(jnp.tile(jnp.arange(1, D_STATE + 1, dtype=jnp.float32)[None, :], (D_INNER, 1)))
        inp = {'hidden_states': jax.random.normal(ks[0], (BATCH, SEQLEN, D_MODEL), jnp.float32), 'in_proj_w': jax.random.normal(ks[1], (2 * D_INNER, D_MODEL), jnp.float32) * s_in, 'conv_w': jax.random.normal(ks[2], (D_INNER, 1, D_CONV), jnp.float32) * 0.3, 'conv_bias': jnp.zeros((D_INNER,), jnp.float32), 'x_proj_w': jax.random.normal(ks[3], (DT_RANK + 2 * D_STATE, D_INNER), jnp.float32) * s_x, 'dt_proj_w': jax.random.uniform(ks[4], (D_INNER, DT_RANK), jnp.float32, -dt_std, dt_std), 'dt_proj_bias': dt_bias_init(ks[5]), 'A_log': A_log, 'D_skip': jnp.ones((D_INNER,), jnp.float32), 'convb_w': jax.random.normal(ks[6], (D_INNER, 1, D_CONV), jnp.float32) * 0.3, 'convb_bias': jnp.zeros((D_INNER,), jnp.float32), 'x_proj_b_w': jax.random.normal(ks[7], (DT_RANK + 2 * D_STATE, D_INNER), jnp.float32) * s_x, 'dt_proj_b_w': jax.random.uniform(ks[8], (D_INNER, DT_RANK), jnp.float32, -dt_std, dt_std), 'dt_proj_b_bias': dt_bias_init(ks[9]), 'A_b_log': A_log, 'D_b_skip': jnp.ones((D_INNER,), jnp.float32), 'out_proj_w': jax.random.normal(ks[10], (D_MODEL, D_INNER), jnp.float32) * s_x}
        return inp
    _L0_attn_in = _L0_attn_setup()

    def _L0_ffn_setup():
        import jax, jax.numpy as jnp
        import numpy as np
        IN_FEATURES = 128
        ACT_BITS = 4

        def _hadamard(size: int) -> np.ndarray:
            h = np.array([[1.0]], dtype=np.float64)
            while h.shape[0] < size:
                h = np.block([[h, h], [h, -h]])
            return (h / np.sqrt(size)).astype(np.float32)

        def _quantize_activations(x, bits=ACT_BITS):
            pos = 2 ** (bits - 1) - 1
            neg = 2 ** (bits - 1)
            scale = jnp.clip(jnp.max(jnp.abs(jax.lax.stop_gradient(x)), axis=-1, keepdims=True), 1e-05) / pos
            q = jnp.clip(jnp.round(x / scale), -neg, pos) * scale
            return x + jax.lax.stop_gradient(q - x)

        def _ternary_quantize_ste(w):
            scale = jnp.clip(jnp.mean(jnp.abs(jax.lax.stop_gradient(w)), axis=1, keepdims=True), 1e-05)
            n = w / scale
            tern = jnp.where(n > 0.5, 1.0, jnp.where(n < -0.5, -1.0, 0.0))
            q = tern * scale
            return w + jax.lax.stop_gradient(q - w)
        key = jax.random.key(seed)
        k1, k2 = jax.random.split(key)
        x = jax.random.normal(k1, (8, 1024, IN_FEATURES), dtype=jnp.float32)
        bound = 1.0 / np.sqrt(IN_FEATURES)
        weight = jax.random.uniform(k2, (128, IN_FEATURES), dtype=jnp.float32, minval=-bound, maxval=bound)
        return {'x': x, 'weight': weight}
    _L0_ffn_in = _L0_ffn_setup()
    _d = {'L0_attn_hidden_states': _L0_attn_in['hidden_states'], 'L0_attn_in_proj_w': _L0_attn_in['in_proj_w'], 'L0_attn_conv_w': _L0_attn_in['conv_w'], 'L0_attn_conv_bias': _L0_attn_in['conv_bias'], 'L0_attn_x_proj_w': _L0_attn_in['x_proj_w'], 'L0_attn_dt_proj_w': _L0_attn_in['dt_proj_w'], 'L0_attn_dt_proj_bias': _L0_attn_in['dt_proj_bias'], 'L0_attn_A_log': _L0_attn_in['A_log'], 'L0_attn_D_skip': _L0_attn_in['D_skip'], 'L0_attn_convb_w': _L0_attn_in['convb_w'], 'L0_attn_convb_bias': _L0_attn_in['convb_bias'], 'L0_attn_x_proj_b_w': _L0_attn_in['x_proj_b_w'], 'L0_attn_dt_proj_b_w': _L0_attn_in['dt_proj_b_w'], 'L0_attn_dt_proj_b_bias': _L0_attn_in['dt_proj_b_bias'], 'L0_attn_A_b_log': _L0_attn_in['A_b_log'], 'L0_attn_D_b_skip': _L0_attn_in['D_b_skip'], 'L0_attn_out_proj_w': _L0_attn_in['out_proj_w'], 'L0_ffn_weight': _L0_ffn_in['weight']}
    _x0 = _d['L0_attn_hidden_states']
    _d['L0_attn_hidden_states'] = jax.random.normal(jax.random.fold_in(jax.random.key(seed), 1), (8, 512, 128), dtype=_x0.dtype)
    del _x0
    return _d

def reference(L0_attn_hidden_states, L0_attn_in_proj_w, L0_attn_conv_w, L0_attn_conv_bias, L0_attn_x_proj_w, L0_attn_dt_proj_w, L0_attn_dt_proj_bias, L0_attn_A_log, L0_attn_D_skip, L0_attn_convb_w, L0_attn_convb_bias, L0_attn_x_proj_b_w, L0_attn_dt_proj_b_w, L0_attn_dt_proj_b_bias, L0_attn_A_b_log, L0_attn_D_b_skip, L0_attn_out_proj_w, L0_ffn_weight):

    def _L0_attn_ref(hidden_states, in_proj_w, conv_w, conv_bias, x_proj_w, dt_proj_w, dt_proj_bias, A_log, D_skip, convb_w, convb_bias, x_proj_b_w, dt_proj_b_w, dt_proj_b_bias, A_b_log, D_b_skip, out_proj_w):
        import jax, jax.numpy as jnp
        import numpy as np
        D_MODEL = 128
        D_STATE = 16
        D_CONV = 4
        EXPAND = 2
        D_INNER = EXPAND * D_MODEL
        DT_RANK = (D_MODEL + 15) // 16
        BATCH = 2
        SEQLEN = 128

        def _causal_conv_silu(x, w, b):
            k = w.shape[-1]
            y = jax.lax.conv_general_dilated(x, w, window_strides=(1,), padding=[(k - 1, 0)], dimension_numbers=('NCH', 'OIH', 'NCH'), feature_group_count=x.shape[1])
            return jax.nn.silu(y + b[None, :, None])

        def _ssm_scan(dA, dBx):

            def op(e1, e2):
                a1, b1 = e1
                a2, b2 = e2
                return (a1 * a2, a2 * b1 + b2)
            return jax.lax.associative_scan(op, (dA, dBx), axis=2)[1]

        def _mamba_dir(xz, conv_w, conv_b, xproj_w, dtproj_w, dt_bias, A_log, Dp):
            d_inner = xz.shape[1] // 2
            x, z = (xz[:, :d_inner], xz[:, d_inner:])
            u = _causal_conv_silu(x, conv_w, conv_b)
            x_dbl = jnp.einsum('bdl,kd->bkl', u, xproj_w)
            n = A_log.shape[1]
            r = dtproj_w.shape[1]
            delta = jnp.einsum('dr,brl->bdl', dtproj_w, x_dbl[:, :r])
            Bm = x_dbl[:, r:r + n]
            Cm = x_dbl[:, r + n:]
            delta = jax.nn.softplus(delta + dt_bias[None, :, None])
            A = -jnp.exp(A_log)
            dA = jnp.exp(jnp.einsum('bdl,dn->bdln', delta, A))
            dBx = jnp.einsum('bdl,bnl,bdl->bdln', delta, Bm, u)
            h = _ssm_scan(dA, dBx)
            y = jnp.einsum('bdln,bnl->bdl', h, Cm)
            y = y + Dp[None, :, None] * u
            return y * jax.nn.silu(z)
        xz = jnp.einsum('ed,bld->bel', in_proj_w, hidden_states)
        out_f = _mamba_dir(xz, conv_w, conv_bias, x_proj_w, dt_proj_w, dt_proj_bias, A_log, D_skip)
        out_b = _mamba_dir(xz[:, :, ::-1], convb_w, convb_bias, x_proj_b_w, dt_proj_b_w, dt_proj_b_bias, A_b_log, D_b_skip)[:, :, ::-1]
        return jnp.einsum('bdl,od->blo', out_f + out_b, out_proj_w)

    def _L0_ffn_ref(x, weight):
        import jax, jax.numpy as jnp
        import numpy as np
        IN_FEATURES = 128
        ACT_BITS = 4

        def _hadamard(size: int) -> np.ndarray:
            h = np.array([[1.0]], dtype=np.float64)
            while h.shape[0] < size:
                h = np.block([[h, h], [h, -h]])
            return (h / np.sqrt(size)).astype(np.float32)

        def _quantize_activations(x, bits=ACT_BITS):
            pos = 2 ** (bits - 1) - 1
            neg = 2 ** (bits - 1)
            scale = jnp.clip(jnp.max(jnp.abs(jax.lax.stop_gradient(x)), axis=-1, keepdims=True), 1e-05) / pos
            q = jnp.clip(jnp.round(x / scale), -neg, pos) * scale
            return x + jax.lax.stop_gradient(q - x)

        def _ternary_quantize_ste(w):
            scale = jnp.clip(jnp.mean(jnp.abs(jax.lax.stop_gradient(w)), axis=1, keepdims=True), 1e-05)
            n = w / scale
            tern = jnp.where(n > 0.5, 1.0, jnp.where(n < -0.5, -1.0, 0.0))
            q = tern * scale
            return w + jax.lax.stop_gradient(q - w)
        H = jnp.asarray(_hadamard(IN_FEATURES))
        xh = x @ H
        xq = _quantize_activations(xh)
        wq = _ternary_quantize_ste(weight)
        return jnp.einsum('bsi,oi->bso', xq, wq)
    x = L0_attn_hidden_states
    xn = _layernorm(x, axis=-1)
    x = x + _L0_attn_ref(xn, L0_attn_in_proj_w, L0_attn_conv_w, L0_attn_conv_bias, L0_attn_x_proj_w, L0_attn_dt_proj_w, L0_attn_dt_proj_bias, L0_attn_A_log, L0_attn_D_skip, L0_attn_convb_w, L0_attn_convb_bias, L0_attn_x_proj_b_w, L0_attn_dt_proj_b_w, L0_attn_dt_proj_b_bias, L0_attn_A_b_log, L0_attn_D_b_skip, L0_attn_out_proj_w) + _L0_ffn_ref(xn, L0_ffn_weight)
    return x

_drawn_inputs = setup_inputs


def setup_inputs(seed=0):
    import zlib

    import numpy as np

    out = dict(_drawn_inputs(seed))
    spreads = {'L0_attn_conv_bias': (0.0, 0.1),
     'L0_attn_D_skip': (1.0, 0.6),
     'L0_attn_convb_bias': (0.0, 0.1),
     'L0_attn_D_b_skip': (1.0, 0.6)}
    factors = {'L0_attn_x_proj_w': 7.299,
     'L0_attn_dt_proj_w': 8.0,
     'L0_attn_dt_proj_bias': 8.0,
     'L0_attn_A_log': 8.0,
     'L0_attn_x_proj_b_w': 7.792,
     'L0_attn_dt_proj_b_w': 8.0,
     'L0_attn_dt_proj_b_bias': 8.0,
     'L0_attn_A_b_log': 8.0,
     'L0_ffn_weight': 4.382}
    for name, (base, spread) in spreads.items():
        noise = np.random.default_rng([zlib.crc32(name.encode()), seed]).standard_normal(out[name].shape)
        drawn = base * np.exp(spread * noise) if base else spread * noise
        out[name] = jnp.asarray(drawn.astype(out[name].dtype))
    for name, factor in factors.items():
        out[name] = (out[name] * factor).astype(out[name].dtype)
    return out
```

```python
from contextlib import ExitStack

import numpy as np

import concourse.bass as bass
from concourse import mybir

F32 = mybir.dt.float32
ALU = mybir.AluOpType
ACT = mybir.ActivationFunctionType
AX = mybir.AxisListType

P = 128
NB, L, DM = 8, 512, 128
DI, NS, DR, TAPS = 256, 16, 8, 4
NH = DI // P
CB = 32
NJ = P // CB
NR = P // CB
NQ = NS // NR
SLOTS = NH * NQ
PER_B = 2 * SLOTS
NC = L // P
PAD = TAPS - 1
LN_EPS, Q_FLOOR, Q_POS, Q_NEG = 1e-5, 1e-5, 7.0, 8.0
ROUND = 12582912.0
DMA = 16
XC = 64
REP_DMAS = NJ * NR


def build(nc, x, win_t, wz_t, conv_w, cols, xproj_t, dt_t, a_log, wout_t, ffn_w, had, ident_d, sum_sel_d, rep_sel_d, out):
    ctx = ExitStack()
    with ctx:
        def sb(name, shape):
            return ctx.enter_context(nc.sbuf_tensor(name, shape, F32))

        def sem(name):
            return ctx.enter_context(nc.semaphore(name))

        conv_wt = [sb(f"conv_wt{d}", [P, TAPS, DI]) for d in range(2)]
        wz = sb("wz", [P, DI])
        col = sb("col", [P, 2, 3, NH])
        half_bias = sb("half_bias", [P, 2, NH])
        xproj = [sb(f"xproj{d}", [P, NH, XC]) for d in range(2)]
        dtw = [sb(f"dtw{d}", [P, DI]) for d in range(2)]
        neg_a = sb("neg_a", [P, 2, NH, NJ, NQ])
        skip = sb("skip", [P, 2, NH, P])
        wout = sb("wout", [P, NH, DM])
        wq_t = sb("wq_t", [P, DM])
        fcol = sb("fcol", [P, 4])
        hadm = sb("hadm", [P, DM])
        ident = sb("ident", [P, P])
        sum_sel = sb("sum_sel", [P, CB])
        rep_sel = sb("rep_sel", [P, 2 * NQ, P])
        x_ln = sb("x_ln", [P, NC, DM])
        x_res = sb("x_res", [P, NC, DM])
        stats = sb("stats", [P, NC, 6])
        msum = sb("msum", [P, NC])
        mdiff = sb("mdiff", [P, NC])
        rstd = sb("rstd", [P, NC])
        var = sb("var", [P, NC])
        shift = sb("shift", [P, NC])
        xn = sb("xn", [P, NC, DM])
        xnt = [sb(f"xnt{d}", [P, PAD + L]) for d in range(2)]
        amax = sb("amax", [P, NC])
        qscale = sb("qscale", [P, NC])
        qinv = sb("qinv", [P, NC])
        xq = sb("xq", [P, NC, DM])
        xqt = sb("xqt", [P, L])
        gate = sb("gate", [P, NH, L])
        y_gated = sb("y_gated", [P, NH, L])
        u = [sb(f"u{d}", [P, NH, L]) for d in range(2)]
        xdbl = [sb(f"xdbl{d}", [P, L]) for d in range(2)]
        t_exp = sb("t_exp", [P, NH, L])
        t_log = sb("t_log", [P, NH, L])
        t_pos = sb("t_pos", [P, NH, L])
        t_cor = sb("t_cor", [P, NH, L])
        dd = [sb(f"dd{h}", [P, 2, L]) for h in range(NH)]
        rep = [[sb(f"rep{d}{h}", [P, 2, NJ, L]) for h in range(NH)] for d in range(2)]
        b_rep = [sb(f"b_rep{d}", [P, NQ, L]) for d in range(2)]
        c_rep = [sb(f"c_rep{d}", [P, NQ, L]) for d in range(2)]
        dbx = [sb(f"dbx{n}", [P, NJ, L]) for n in range(2)]
        hst = [sb(f"hst{n}", [P, NJ, L]) for n in range(2)]
        da = ctx.enter_context(nc.psum_tensor("da", [P, NJ, L], F32))
        y = ctx.enter_context(nc.psum_tensor("y", [P, NH, L], F32))
        pb = ctx.enter_context(nc.psum_tensor("pb", [P, 2, L], F32))

        w_loaded = sem("w_loaded")
        conv_loaded = sem("conv_loaded")
        zeroed = sem("zeroed")
        a_exp = sem("a_exp")
        set_step = sem("set_step")
        fw_ready = sem("fw_ready")
        fwt_filled = sem("fwt_filled")
        fwt_read = sem("fwt_read")
        weights_ready = sem("weights_ready")
        x_loaded = sem("x_loaded")
        xres_loaded = sem("xres_loaded")
        ln_step = sem("ln_step")
        rstd_guess = sem("rstd_guess")
        xn_ready = sem("xn_ready")
        xnt_filled = sem("xnt_filled")
        xnt_ready = sem("xnt_ready")
        had_filled = sem("had_filled")
        q_step = sem("q_step")
        had_read = sem("had_read")
        xq_ready = sem("xq_ready")
        xqt_filled = sem("xqt_filled")
        xqt_ready = sem("xqt_ready")
        z_filled = sem("z_filled")
        z_step = sem("z_step")
        z_sig = sem("z_sig")
        gate_ready = sem("gate_ready")
        conv_filled = sem("conv_filled")
        u_step = sem("u_step")
        u_sig = sem("u_sig")
        u_ready = sem("u_ready")
        xdbl_filled = sem("xdbl_filled")
        xdbl_ready = sem("xdbl_ready")
        dt_filled = sem("dt_filled")
        sp_step = sem("sp_step")
        dt_read = sem("dt_read")
        t_ready = sem("t_ready")
        cor_step = sem("cor_step")
        delta_done = sem("delta_done")
        dd_ready = sem("dd_ready")
        rep_loaded = [[sem(f"rep_loaded{d}{h}") for h in range(NH)] for d in range(2)]
        bc_filled = sem("bc_filled")
        bc_ready = sem("bc_ready")
        decay_done = sem("decay_done")
        input_done = sem("input_done")
        scan_done = sem("scan_done")
        prod_done = sem("prod_done")
        sum_done = sem("sum_done")
        y_read = sem("y_read")
        out_filled = sem("out_filled")
        out_ready = sem("out_ready")
        out_stored = sem("out_stored")

        block = ctx.enter_context(nc.Block())

        def wait(eng, s, count):
            if not isinstance(count, int) or count > 0:
                eng.wait_ge(s, count)

        BC = [("b", 0), ("b", 1), ("b", 2), ("c", 0), ("c", 1), ("c", 2), ("b", 3), ("c", 3)]
        BC_BANK = [[1, 0, 1, 0, 1, 0, 1, 0], [0, 0, 0, 1, 0, 1, 1, 0]]
        BC_AT = {bc: n + 1 for n, bc in enumerate(BC)}

        def batches(eng, body):
            body(0)
            with eng.Fori(1, NB - 1) as i:
                body(i)
            body(NB - 1)

        def first(b):
            return isinstance(b, int) and b == 0

        def last(b):
            return isinstance(b, int) and b == NB - 1

        @block.sync
        def _(sp):
            def rows(ap, b):
                return ap[bass.ds(b, 1)].rearrange("b (c p) d -> p (b c) d", p=P)

            def load_x(b):
                src = rows(x, b)
                wait(sp, xn_ready, b)
                sp.dma_start(x_ln[:, :, :], src).then_inc(x_loaded, DMA)

            def load_res(b):
                wait(sp, out_stored, DMA * b)
                sp.dma_start(x_res[:, :, :], rows(x, b)).then_inc(xres_loaded, DMA)

            def store_out(b):
                wait(sp, out_ready, b + 1)
                sp.dma_start(rows(out, b), x_res[:, :, :]).then_inc(out_stored, DMA)

            def spread(d, V):
                for h in range(NH):
                    wait(sp, dd_ready, 2 * V + h + 1)
                    for r in range(NR):
                        for j in range(NJ):
                            sp.dma_start(rep[d][h][CB * r:CB * (r + 1), :, j, :],
                                         dd[h][CB * j:CB * (j + 1), :, :]).then_inc(rep_loaded[d][h], DMA)

            load_x(0)
            for d in range(2):
                sp.dma_start(conv_wt[d][:, :, :], conv_w[d:d + 1].broadcast_to([P, TAPS, DI])).then_inc(conv_loaded, DMA)
            sp.dma_start(wz[:, :], wz_t).then_inc(w_loaded, DMA)
            sp.dma_start(col[:, :, :, :], cols).then_inc(w_loaded, DMA)
            sp.dma_start(neg_a[:, :, :, :, :], a_log).then_inc(w_loaded, DMA)
            sp.dma_start(wout[:, :, :], wout_t).then_inc(w_loaded, DMA)
            sp.dma_start(hadm[:, :], had).then_inc(w_loaded, DMA)
            sp.dma_start(sum_sel[:, :], sum_sel_d).then_inc(w_loaded, DMA)
            sp.dma_start(rep_sel[:, :, :], rep_sel_d).then_inc(w_loaded, DMA)
            sp.wait_ge(zeroed, 4)
            for d in range(2):
                sp.dma_start(xproj[d][:, :, 0:DR + 2 * NS], xproj_t[d]).then_inc(w_loaded, DMA)
                sp.dma_start(dtw[d][0:DR, :], dt_t[d]).then_inc(w_loaded, DMA)
            spread(0, 0)

            def body(b):
                if not last(b):
                    load_x(b + 1)
                if not first(b):
                    store_out(b - 1)
                load_res(b)
                spread(1, 2 * b + 1)
                if not last(b):
                    spread(0, 2 * b + 2)

            batches(sp, body)
            store_out(NB - 1)
            sp.wait_ge(out_stored, DMA * NB)

        W_LOADS = 7 + 4
        WIN = hst[0][:, 0, 0:DI]
        fw = t_cor[:, 0, 0:DM]
        ft = t_cor[:, 0, DM:2 * DM]

        @block.scalar
        def _(act):
            act.dma_start(WIN, win_t).then_inc(conv_loaded, DMA)
            act.dma_start(fw, ffn_w).then_inc(conv_loaded, DMA)
            act.dma_start(ident[:, :], ident_d).then_inc(conv_loaded, DMA)

            def log_var(b):
                act.wait_ge(ln_step, 15 * b + 10)
                nc.scalar.activation(rstd[:, :], var[:, :], ACT.Ln).then_inc(rstd_guess, 1)

            def guess_rstd(b):
                act.wait_ge(rstd_guess, 2 * b + 1)
                nc.scalar.activation(rstd[:, :], rstd[:, :], ACT.Exp, scale=-0.5).then_inc(rstd_guess, 1)

            def normalize(b):
                wait(act, ln_step, 15 * b + 15)
                wait(act, xnt_filled, b)
                for c in range(NC):
                    ins = nc.scalar.activation(xn[:, c, :], x_ln[:, c, :], ACT.Identity, bias=shift[:, c:c + 1], scale=rstd[:, c:c + 1])
                ins.then_inc(xn_ready, 1)

            def keep_xnt(b):
                wait(act, xnt_filled, b + 1)
                wait(act, z_filled, 2 * b)
                nc.scalar.activation(xnt[0][:, PAD:PAD + L], pb[:, 1, :], ACT.Copy).then_inc(xnt_ready, 1)
                nc.scalar.activation(xnt[1][:, PAD:PAD + L], pb[:, 1, ::-1], ACT.Copy).then_inc(xnt_ready, 1)

            def keep_xqt(b):
                wait(act, xqt_filled, b + 1)
                wait(act, out_filled, b)
                nc.scalar.activation(xqt[:, :], pb[:, 1, :], ACT.Copy).then_inc(xqt_ready, 1)

            def u_tanh(d, V, h):
                wait(act, conv_filled, 2 * V + h + 1)
                wait(act, dd_ready, 2 * V)
                nc.scalar.activation(t_exp[:, h, :], pb[:, h, :], ACT.Tanh, bias=half_bias[:, d, h:h + 1], scale=0.5).then_inc(u_step, 1)

            def u_sigmoid(V):
                act.wait_ge(u_step, 2 * V + 2)
                nc.scalar.activation(t_exp[:, :, :], t_exp[:, :, :], ACT.Copy, bias=0.5, scale=0.5).then_inc(u_sig, 1)

            def z_sigmoid(b):
                wait(act, y_read, 2 * b)
                for h in range(NH):
                    act.wait_ge(z_filled, 2 * b + h + 1)
                    nc.scalar.activation(gate[:, h, :], pb[:, 1 - h, :], ACT.Tanh, scale=0.5).then_inc(z_step, 1)
                act.wait_ge(z_step, 2 * b + 2)
                nc.scalar.activation(gate[:, :, :], gate[:, :, :], ACT.Copy, bias=0.5, scale=0.5).then_inc(z_sig, 1)

            def keep_xdbl(d, V):
                wait(act, xdbl_filled, V + 1)
                wait(act, bc_filled, 8 * V - 8)
                nc.scalar.activation(xdbl[d][0:XC, :], pb[0:XC, 0, :], ACT.Copy).then_inc(xdbl_ready, 1)

            def softplus_exp(d, V):
                wait(act, u_ready, 2 * V + 2)
                for h in range(NH):
                    act.wait_ge(dt_filled, 2 * V + h + 1)
                    nc.scalar.activation(t_exp[:, h, :], pb[:, 1 - h, :], ACT.Abs, bias=col[:, d, 1, h:h + 1]).then_inc(sp_step, 1)
                act.wait_ge(sp_step, 4 * V + 2)
                nc.scalar.activation(t_exp[:, :, :], t_exp[:, :, :], ACT.Exp, scale=-1.0).then_inc(sp_step, 1)

            def softplus_log(d, V):
                wait(act, delta_done, 2 * V)
                for h in range(NH):
                    nc.scalar.activation(t_pos[:, h, :], pb[:, 1 - h, :], ACT.Relu, bias=col[:, d, 1, h:h + 1]).then_inc(dt_read, 1)
                act.wait_ge(sp_step, 4 * V + 3)
                nc.scalar.activation(t_cor[:, :, :], t_exp[:, :, :], ACT.Copy, bias=1.0).then_inc(sp_step, 1)
                act.wait_ge(sp_step, 4 * V + 4)
                nc.scalar.activation(t_log[:, :, :], t_cor[:, :, :], ACT.Ln).then_inc(t_ready, 1)

            def keep_bc(d, V, n):
                kind, q = BC[n]
                act.wait_ge(bc_filled, 8 * V + n + 1)
                if n == 0:
                    wait(act, input_done, SLOTS * (V - 1))
                    wait(act, prod_done, 2 * SLOTS * (V - 1))
                dst = b_rep if kind == "b" else c_rep
                nc.scalar.activation(dst[d][:, q, :], pb[:, BC_BANK[d][n], :], ACT.Copy).then_inc(bc_ready, 1)

            def decays(b, d, s, p):
                S = PER_B * b + SLOTS * d + s
                h, q = divmod(s, NQ)
                if p == 0 and q == 0:
                    wait(act, rep_loaded[d][h], DMA * REP_DMAS * (b + 1))
                wait(act, scan_done, 2 * S + p - 1)
                for j in (2 * p, 2 * p + 1):
                    ins = nc.scalar.activation(da[:, j, 1:L], rep[d][h][:, 0, j, 1:L], ACT.Exp, scale=neg_a[:, d, h, j, q:q + 1])
                ins.then_inc(decay_done, 1)

            act.wait_ge(w_loaded, DMA * W_LOADS)
            nc.scalar.activation(neg_a[:, :, :, :, :], neg_a[:, :, :, :, :], ACT.Exp).then_inc(a_exp, 1)
            log_var(0)
            guess_rstd(0)
            normalize(0)
            keep_xnt(0)
            act.wait_ge(weights_ready, 3)
            u_tanh(0, 0, 0)
            u_tanh(0, 0, 1)
            u_sigmoid(0)
            keep_xdbl(0, 0)
            softplus_exp(0, 0)
            softplus_log(0, 0)
            for n in range(6):
                keep_bc(0, 0, n)

            def unit(b, d):
                U = 2 * b + d
                V, e = U + 1, 1 - d
                nxt = d == 0 or not last(b)
                nb = d == 0 and not last(b)
                for s in range(SLOTS):
                    decays(b, d, s, 0)
                    if s == 0 and nxt:
                        u_tanh(e, V, 0)
                    if s == 6 and nb:
                        keep_xnt(b + 1)
                    if s == 3 and nxt:
                        softplus_log(e, V)
                    if s == 3 and nb:
                        log_var(b + 1)
                        guess_rstd(b + 1)
                    if s == 4 and nb:
                        normalize(b + 1)
                    decays(b, d, s, 1)
                    if s == 0 and nxt:
                        u_tanh(e, V, 1)
                        u_sigmoid(V)
                    if s == 1:
                        if nxt:
                            keep_xdbl(e, V)
                        keep_bc(d, U, 6)
                        keep_bc(d, U, 7)
                    if s == 2 and nxt:
                        softplus_exp(e, V)
                    if d == 0:
                        if s == 3:
                            keep_bc(e, V, 0)
                        if s == 4:
                            z_sigmoid(b)
                        if s == 5:
                            keep_bc(e, V, 1)
                        if s == 6:
                            keep_xqt(b)
                            keep_bc(e, V, 2)
                            keep_bc(e, V, 3)
                        if s == 7:
                            keep_bc(e, V, 4)
                            keep_bc(e, V, 5)
                    elif nxt and s in (3, 4, 5):
                        keep_bc(e, V, 2 * s - 6)
                        keep_bc(e, V, 2 * s - 5)

            def body(b):
                unit(b, 0)
                unit(b, 1)

            batches(act, body)

        @block.vector
        def _(dve):
            def statistics(b):
                dve.wait_ge(x_loaded, DMA * (b + 1))
                wait(dve, xn_ready, b)
                for c in range(NC):
                    nc.vector.bn_stats(stats[:, c, :], x_ln[:, c, :]).then_inc(ln_step, 1)
                dve.wait_ge(ln_step, 15 * b + 4)
                nc.vector.tensor_tensor(msum[:, :], stats[:, :, 1], stats[:, :, 4], ALU.add).then_inc(ln_step, 1)
                nc.vector.tensor_tensor(mdiff[:, :], stats[:, :, 1], stats[:, :, 4], ALU.subtract).then_inc(ln_step, 1)
                nc.vector.tensor_tensor(var[:, :], stats[:, :, 2], stats[:, :, 5], ALU.add).then_inc(ln_step, 1)
                dve.wait_ge(ln_step, 15 * b + 7)
                nc.vector.scalar_tensor_tensor(mdiff[:, :], mdiff[:, :], 0.25, mdiff[:, :], ALU.mult, ALU.mult).then_inc(ln_step, 1)
                nc.vector.tensor_scalar(var[:, :], var[:, :], 1.0 / DM, LN_EPS, ALU.mult, ALU.add).then_inc(ln_step, 1)
                dve.wait_ge(ln_step, 15 * b + 9)
                nc.vector.tensor_tensor(var[:, :], var[:, :], mdiff[:, :], ALU.add).then_inc(ln_step, 1)

            def refine(b):
                dve.wait_ge(rstd_guess, 2 * b + 2)
                nc.vector.tensor_tensor(shift[:, :], rstd[:, :], rstd[:, :], ALU.mult).then_inc(ln_step, 1)
                dve.wait_ge(ln_step, 15 * b + 11)
                nc.vector.tensor_tensor(shift[:, :], shift[:, :], var[:, :], ALU.mult).then_inc(ln_step, 1)
                dve.wait_ge(ln_step, 15 * b + 12)
                nc.vector.tensor_scalar(shift[:, :], shift[:, :], -0.5, 1.5, ALU.mult, ALU.add).then_inc(ln_step, 1)
                dve.wait_ge(ln_step, 15 * b + 13)
                nc.vector.tensor_tensor(rstd[:, :], rstd[:, :], shift[:, :], ALU.mult).then_inc(ln_step, 1)
                dve.wait_ge(ln_step, 15 * b + 14)
                nc.vector.scalar_tensor_tensor(shift[:, :], msum[:, :], -0.5, rstd[:, :], ALU.mult, ALU.mult).then_inc(ln_step, 1)

            def quantize(b):
                dve.wait_ge(had_filled, b + 1)
                wait(dve, xqt_filled, b)
                xh = pb[:, 1, :].rearrange("p (c i) -> p c i", c=NC)
                nc.vector.tensor_reduce(amax[:, :], xh, AX.X, ALU.max, apply_absolute_value=True).then_inc(q_step, 1)
                dve.wait_ge(q_step, 6 * b + 1)
                nc.vector.tensor_scalar(amax[:, :], amax[:, :], Q_FLOOR, None, ALU.max).then_inc(q_step, 1)
                dve.wait_ge(q_step, 6 * b + 2)
                nc.vector.tensor_scalar(qscale[:, :], amax[:, :], 1.0 / Q_POS, None, ALU.mult).then_inc(q_step, 1)
                nc.vector.reciprocal(qinv[:, :], amax[:, :]).then_inc(q_step, 1)
                dve.wait_ge(q_step, 6 * b + 4)
                nc.vector.tensor_scalar(qinv[:, :], qinv[:, :], Q_POS, None, ALU.mult).then_inc(q_step, 1)
                dve.wait_ge(q_step, 6 * b + 5)
                for c in range(NC):
                    ins = nc.vector.tensor_scalar(xq[:, c, :], xh[:, c, :], qinv[:, c:c + 1], ROUND, ALU.mult, ALU.add)
                ins.then_inc(had_read, 1)
                dve.wait_ge(had_read, b + 1)
                nc.vector.tensor_scalar(xq[:, :, :], xq[:, :, :], ROUND, Q_POS, ALU.subtract, ALU.min).then_inc(q_step, 1)
                dve.wait_ge(q_step, 6 * b + 6)
                for c in range(NC):
                    ins = nc.vector.tensor_scalar(xq[:, c, :], xq[:, c, :], -Q_NEG, qscale[:, c:c + 1], ALU.max, ALU.mult)
                ins.then_inc(xq_ready, 1)

            def gates(b):
                dve.wait_ge(z_sig, b + 1)
                for h in range(NH):
                    nc.vector.tensor_tensor(gate[:, h, :], pb[:, 1 - h, :], gate[:, h, :], ALU.mult).then_inc(gate_ready, 1)

            def make_u(d, V):
                dve.wait_ge(u_sig, V + 1)
                wait(dve, sum_done, SLOTS * (V - 1))
                for h in range(NH):
                    nc.vector.scalar_tensor_tensor(u[d][:, h, :], pb[:, h, :], col[:, d, 0, h:h + 1], t_exp[:, h, :], ALU.add, ALU.mult).then_inc(u_ready, 1)

            def log1p(V):
                dve.wait_ge(t_ready, V + 1)
                nc.vector.scalar_tensor_tensor(t_cor[:, :, :], t_cor[:, :, :], 1.0, t_log[:, :, :], ALU.subtract, ALU.subtract).then_inc(cor_step, 1)
                dve.wait_ge(cor_step, 2 * V + 1)
                nc.vector.scalar_tensor_tensor(t_cor[:, :, :], t_cor[:, :, :], 0.0, t_exp[:, :, :], ALU.max, ALU.subtract).then_inc(cor_step, 1)

            def delta_u(d, V):
                for h in range(NH):
                    dve.wait_ge(delta_done, 2 * V + h + 1)
                    nc.vector.tensor_tensor(dd[h][:, 1, :], dd[h][:, 0, :], u[d][:, h, :], ALU.mult).then_inc(dd_ready, 1)

            def scan_input(b, d, s):
                S = PER_B * b + SLOTS * d + s
                h, q = divmod(s, NQ)
                dve.wait_ge(bc_ready, 8 * (2 * b + d) + BC_AT["b", q])
                if q == 0:
                    dve.wait_ge(rep_loaded[d][h], DMA * REP_DMAS * (b + 1))
                wait(dve, scan_done, 2 * (S - 1))
                nc.vector.tensor_tensor(dbx[s % 2][:, :, :], rep[d][h][:, 1, :, :], b_rep[d][:, q:q + 1, :].broadcast_to([P, NJ, L]), ALU.mult).then_inc(input_done, 1)

            def scan(b, d, s, p):
                S = PER_B * b + SLOTS * d + s
                dve.wait_ge(decay_done, 2 * S + p + 1)
                if p == 0:
                    dve.wait_ge(input_done, S + 1)
                    wait(dve, sum_done, S - 1)
                two = slice(2 * p, 2 * p + 2)
                nc.vector.tensor_tensor_scan(hst[s % 2][:, two, :].rearrange("p j l -> p (j l)"),
                                             da[:, two, :].rearrange("p j l -> p (j l)"),
                                             dbx[s % 2][:, two, :].rearrange("p j l -> p (j l)"),
                                             0.0, ALU.mult, ALU.add).then_inc(scan_done, 1)

            def gate_y(b, h):
                dve.wait_ge(sum_done, PER_B * b + SLOTS + NQ * (h + 1))
                dve.wait_ge(gate_ready, 2 * b + 2)
                wait(dve, out_filled, b)
                nc.vector.tensor_tensor(y_gated[:, h, :], y[:, h, :], gate[:, h, :], ALU.mult).then_inc(y_read, 1)

            def add_residual(b):
                dve.wait_ge(out_filled, b + 1)
                dve.wait_ge(xres_loaded, DMA * (b + 1))
                nc.vector.tensor_tensor(x_res[:, :, :], y[:, 1, :].rearrange("p (c o) -> p c o", c=NC), x_res[:, :, :], ALU.add).then_inc(out_ready, 1)

            for d in range(2):
                nc.vector.memset(xproj[d][:, :, :], 0.0).then_inc(zeroed, 1)
                nc.vector.memset(dtw[d][:, :], 0.0).then_inc(zeroed, 1)
            for d in range(2):
                nc.vector.memset(xnt[d][:, 0:PAD], 0.0)
                nc.vector.memset(xdbl[d][XC:P, :], 0.0)
            nc.vector.memset(da[:, :, 0:1], 0.0).then_inc(zeroed, 1)
            statistics(0)
            refine(0)
            dve.wait_ge(conv_loaded, DMA * 5)
            for d in range(2):
                nc.vector.tensor_tensor(conv_wt[d][:, :, :], conv_wt[d][:, :, :], hst[0][:, 0:1, 0:DI].broadcast_to([P, TAPS, DI]), ALU.mult).then_inc(weights_ready, 1)
            dve.wait_ge(w_loaded, DMA * W_LOADS)
            nc.vector.tensor_scalar(half_bias[:, :, :], col[:, :, 0, :], 0.5, None, ALU.mult).then_inc(weights_ready, 1)
            for d in range(2):
                for h in range(NH):
                    nc.vector.tensor_scalar(skip[:, d, h, :], ident[:, :], col[:, d, 2, h:h + 1], None, ALU.mult).then_inc(set_step, 1)
            dve.wait_ge(a_exp, 1)
            nc.vector.tensor_scalar(neg_a[:, :, :, :, :], neg_a[:, :, :, :, :], -1.0, None, ALU.mult).then_inc(weights_ready, 1)
            nc.vector.tensor_reduce(fcol[:, 0:1], fw, AX.X, ALU.add, apply_absolute_value=True).then_inc(set_step, 1)
            dve.wait_ge(set_step, 5)
            nc.vector.tensor_scalar(fcol[:, 1:2], fcol[:, 0:1], 1.0 / DM, Q_FLOOR, ALU.mult, ALU.max).then_inc(set_step, 1)
            dve.wait_ge(set_step, 6)
            nc.vector.tensor_scalar(fcol[:, 2:3], fcol[:, 1:2], 0.5, None, ALU.mult).then_inc(set_step, 1)
            nc.vector.tensor_scalar(fcol[:, 3:4], fcol[:, 1:2], -0.5, None, ALU.mult).then_inc(set_step, 1)
            dve.wait_ge(set_step, 8)
            nc.vector.tensor_scalar(ft, fw, fcol[:, 3:4], None, ALU.is_lt).then_inc(set_step, 1)
            dve.wait_ge(set_step, 9)
            nc.vector.scalar_tensor_tensor(ft, fw, fcol[:, 2:3], ft, ALU.is_gt, ALU.subtract).then_inc(set_step, 1)
            dve.wait_ge(set_step, 10)
            nc.vector.tensor_scalar(ft, ft, fcol[:, 1:2], None, ALU.mult).then_inc(fw_ready, 1)
            dve.wait_ge(fwt_filled, 1)
            nc.vector.tensor_copy(wq_t[:, :], pb[:, 0, 0:DM]).then_inc(fwt_read, 1)
            make_u(0, 0)
            log1p(0)
            delta_u(0, 0)
            scan_input(0, 0, 0)

            def unit(b, d):
                U = 2 * b + d
                V, e = U + 1, 1 - d
                nxt = d == 0 or not last(b)
                for s in range(SLOTS):
                    if s < SLOTS - 1:
                        scan_input(b, d, s + 1)
                    elif nxt:
                        scan_input(b + d, e, 0)
                    scan(b, d, s, 0)
                    scan(b, d, s, 1)
                    if s == 0 and nxt:
                        make_u(e, V)
                    if s == 3 and nxt:
                        log1p(V)
                    if s == 4 and nxt:
                        delta_u(e, V)
                    if d == 0:
                        if s == 1 and not first(b):
                            gate_y(b - 1, 1)
                        if s == 2 and not last(b):
                            statistics(b + 1)
                        if s == 3 and not last(b):
                            refine(b + 1)
                        if s == 3 and not first(b):
                            add_residual(b - 1)
                        if s == 4:
                            quantize(b)
                            gates(b)
                    if d == 1 and s == 6:
                        gate_y(b, 0)

            def body(b):
                unit(b, 0)
                unit(b, 1)

            batches(dve, body)
            gate_y(NB - 1, 1)
            add_residual(NB - 1)

        @block.gpsimd
        def _(pool):
            def states_times_c(b, d, s, p):
                S = PER_B * b + SLOTS * d + s
                q = s % NQ
                pool.wait_ge(scan_done, 2 * S + p + 1)
                if p == 0:
                    pool.wait_ge(bc_ready, 8 * (2 * b + d) + BC_AT["c", q])
                two = slice(2 * p, 2 * p + 2)
                nc.gpsimd.tensor_tensor(hst[s % 2][:, two, :], hst[s % 2][:, two, :], c_rep[d][:, q:q + 1, :].broadcast_to([P, 2, L]), ALU.mult).then_inc(prod_done, 1)

            def delta(d, V, b):
                pool.wait_ge(cor_step, 2 * V + 2)
                for h in range(NH):
                    wait(pool, rep_loaded[1 - d][h], DMA * REP_DMAS * (b + d))
                    nc.gpsimd.tensor_tensor(dd[h][:, 0, :], t_pos[:, h, :], t_cor[:, h, :], ALU.subtract).then_inc(delta_done, 1)

            delta(0, 0, 0)

            def unit(b, d):
                for s in range(SLOTS):
                    states_times_c(b, d, s, 0)
                    states_times_c(b, d, s, 1)
                    if s == 3 and (d == 0 or not last(b)):
                        delta(1 - d, 2 * b + d + 1, b + d)

            def body(b):
                unit(b, 0)
                unit(b, 1)

            batches(pool, body)

        @block.tensor
        def _(pe):
            mm = nc.tensor.matmul

            def conv(d, V, h, free, count):
                wait(pe, free, count)
                for k in range(TAPS):
                    ins = mm(pb[:, h, :], conv_wt[d][:, k, P * h:P * (h + 1)], xnt[d][:, k:k + L], start=k == 0, stop=k == TAPS - 1)
                ins.then_inc(conv_filled, 1)

            def x_proj(d, V):
                pe.wait_ge(u_ready, 2 * V + 2)
                for h in range(NH):
                    ins = mm(pb[0:XC, 0, :], xproj[d][:, h, :], u[d][:, h, :], start=h == 0, stop=h == NH - 1)
                ins.then_inc(xdbl_filled, 1)

            def steps(d, V, free, counts):
                pe.wait_ge(xdbl_ready, V + 1)
                for h in range(NH):
                    wait(pe, free, counts[h])
                    mm(pb[:, 1 - h, :], dtw[d][:, P * h:P * (h + 1)], xdbl[d][:, :], start=True, stop=True).then_inc(dt_filled, 1)

            def spread_bc(d, V, n, free, count):
                kind, q = BC[n]
                wait(pe, free, count)
                mm(pb[:, BC_BANK[d][n], :], rep_sel[:, q + NQ * (kind == "c"), :], xdbl[d][:, :], start=True, stop=True).then_inc(bc_filled, 1)

            def transpose_xn(b, free, count):
                wait(pe, xn_ready, b + 1)
                wait(pe, free, count)
                for c in range(NC):
                    ins = nc.tensor.transpose(pb[:, 1, P * c:P * (c + 1)], xn[:, c, :], ident[:, :])
                ins.then_inc(xnt_filled, 1)

            def hadamard(b, free, count):
                wait(pe, free, count)
                for c in range(NC):
                    ins = mm(pb[:, 1, P * c:P * (c + 1)], xnt[0][:, PAD + P * c:PAD + P * (c + 1)], hadm[:, :], start=True, stop=True)
                ins.then_inc(had_filled, 1)

            def transpose_xq(b, free, count):
                pe.wait_ge(xq_ready, b + 1)
                wait(pe, free, count)
                for c in range(NC):
                    ins = nc.tensor.transpose(pb[:, 1, P * c:P * (c + 1)], xq[:, c, :], ident[:, :])
                ins.then_inc(xqt_filled, 1)

            def z_proj(h, free, count):
                wait(pe, free, count)
                mm(pb[:, 1 - h, :], wz[:, P * h:P * (h + 1)], xnt[0][:, PAD:PAD + L], start=True, stop=True).then_inc(z_filled, 1)

            def sum_states(b, d, s):
                S = PER_B * b + SLOTS * d + s
                h, q = divmod(s, NQ)
                step = slice(None, None, -1 if d else 1)
                if q == 0:
                    if d == 0:
                        wait(pe, y_read, 2 * (b - 1) + h + 1)
                        if h == 1:
                            wait(pe, out_ready, b)
                    pe.wait_ge(u_ready, 2 * (2 * b + d) + 2)
                    mm(y[:, h, :], skip[:, d, h, :], u[d][:, h, step], start=d == 0, stop=False, skip_group_check=True)
                pe.wait_ge(prod_done, 2 * S + 2)
                for j in range(NJ):
                    ins = mm(y[CB * j:CB * (j + 1), h, :], sum_sel[:, :], hst[s % 2][:, j, step],
                             start=False, stop=d == 1 and q == NQ - 1, skip_group_check=True)
                ins.then_inc(sum_done, 1)

            def project(b):
                pe.wait_ge(y_read, 2 * b + 2)
                pe.wait_ge(xqt_ready, b + 1)
                for c in range(NC):
                    at = slice(P * c, P * (c + 1))
                    mm(y[:, 1, at], xqt[:, at], wq_t[:, :], start=True, stop=False)
                    for h in range(NH):
                        ins = mm(y[:, 1, at], y_gated[:, h, at], wout[:, h, :], start=False, stop=h == NH - 1)
                ins.then_inc(out_filled, 1)

            pe.wait_ge(conv_loaded, DMA * 5)
            pe.wait_ge(zeroed, 5)
            transpose_xn(0, xn_ready, 1)
            pe.wait_ge(fw_ready, 1)
            nc.tensor.transpose(pb[:, 0, 0:DM], ft, ident[:, :]).then_inc(fwt_filled, 1)
            pe.wait_ge(w_loaded, DMA * W_LOADS)
            pe.wait_ge(weights_ready, 4)
            pe.wait_ge(xnt_ready, 2)
            conv(0, 0, 0, fwt_read, 1)
            conv(0, 0, 1, xnt_ready, 2)
            x_proj(0, 0)
            steps(0, 0, xdbl_ready, (1, 1))
            for n, (free, count) in enumerate([(dt_read, 1), (dt_read, 2)] + [(bc_ready, m) for m in (1, 2, 3, 4)]):
                spread_bc(0, 0, n, free, count)
            conv(1, 1, 0, bc_ready, 6)

            def unit(b, d):
                U = 2 * b + d
                V, e = U + 1, 1 - d
                nxt = d == 0 or not last(b)
                for s in range(SLOTS):
                    if s == 0 and nxt:
                        conv(e, V, 1, bc_ready, 8 * U + (6 if d else 5))
                    if s == 1:
                        if nxt:
                            x_proj(e, V)
                            spread_bc(d, U, 6, u_ready, 2 * V + 2)
                            spread_bc(d, U, 7, xdbl_ready, V + 1)
                        else:
                            spread_bc(d, U, 6, bc_ready, 8 * U + 6)
                            spread_bc(d, U, 7, bc_ready, 8 * U + 6)
                    if s == 2 and nxt:
                        steps(e, V, bc_ready, (8 * U + 7, 8 * U + 8))
                    if d == 0:
                        if s == 3:
                            hadamard(b, dt_read, 2 * V + 1)
                            spread_bc(e, V, 0, dt_read, 2 * V + 2)
                        if s == 4:
                            z_proj(0, had_read, b + 1)
                            z_proj(1, bc_ready, 8 * V + 1)
                        if s == 5:
                            if not last(b):
                                transpose_xn(b + 1, gate_ready, 2 * b + 1)
                            spread_bc(e, V, 1, gate_ready, 2 * b + 2)
                        if s == 6:
                            if last(b):
                                transpose_xq(b, gate_ready, 2 * b + 1)
                            else:
                                transpose_xq(b, xnt_ready, 2 * b + 4)
                            spread_bc(e, V, 2, bc_ready, 8 * V + 2)
                            spread_bc(e, V, 3, xqt_ready, b + 1)
                        if s == 7:
                            spread_bc(e, V, 4, bc_ready, 8 * V + 3)
                            spread_bc(e, V, 5, bc_ready, 8 * V + 4)
                            if not last(b):
                                pe.wait_ge(xnt_ready, 2 * b + 4)
                                conv(0, V + 1, 0, bc_ready, 8 * V + 5)
                    elif nxt:
                        if s in (3, 4, 5):
                            free = [(dt_read, 2 * V + 1), (dt_read, 2 * V + 2)] + [(bc_ready, 8 * V + m) for m in (1, 2, 3, 4)]
                            for n in (2 * s - 6, 2 * s - 5):
                                spread_bc(e, V, n, *free[n])
                        if s == 7:
                            conv(1, V + 1, 0, bc_ready, 8 * V + 6)
                    if s > 0:
                        sum_states(b, d, s - 1)
                    elif d == 1:
                        sum_states(b, 0, SLOTS - 1)
                    elif not first(b):
                        sum_states(b - 1, 1, SLOTS - 1)
                    if d == 0 and s == 2 and not first(b):
                        project(b - 1)

            def body(b):
                unit(b, 0)
                unit(b, 1)

            batches(pe, body)
            sum_states(NB - 1, 1, SLOTS - 1)
            project(NB - 1)


def constants():
    had = np.array([[1.0]])
    while had.shape[0] < DM:
        had = np.block([[had, had], [had, -had]])
    had = (had / np.sqrt(DM)).astype(np.float32)
    ident = np.eye(P, dtype=np.float32)
    sum_sel = np.tile(np.eye(CB, dtype=np.float32), (NR, 1))
    rep_sel = np.zeros((P, 2 * NQ, P), np.float32)
    for g in range(2 * NQ):
        for r in range(NR):
            rep_sel[DR + NR * g + r, g, CB * r:CB * (r + 1)] = 1.0
    return had, ident, sum_sel, rep_sel


def kernel(**inputs):
    import concourse.bacc as bacc
    from concourse.bass_utils import run_bass_kernel_spmd

    v = {k.replace("L0_attn_", ""): np.asarray(a) for k, a in inputs.items()}
    sides = [("conv_w", "conv_bias", "x_proj_w", "dt_proj_w", "dt_proj_bias", "A_log", "D_skip"),
             ("convb_w", "convb_bias", "x_proj_b_w", "dt_proj_b_w", "dt_proj_b_bias", "A_b_log", "D_b_skip")]

    def halves(a):
        return np.moveaxis(a.reshape(NH, P, *a.shape[1:]), 0, 1)

    had, ident, sum_sel, rep_sel = constants()
    arrays = {
        "x": v["hidden_states"],
        "win_t": v["in_proj_w"][:DI].T,
        "wz_t": v["in_proj_w"][DI:].T,
        "conv_w": np.stack([v[s[0]][:, 0, :].T for s in sides]),
        "cols": np.stack([np.stack([halves(v[s[n]]) for n in (1, 4, 6)], 1) for s in sides], 1),
        "xproj_t": np.stack([halves(v[s[2]].T) for s in sides]),
        "dt_t": np.stack([v[s[3]].T for s in sides]),
        "a_log": np.stack([v[s[5]].reshape(NH, NJ, CB, NQ, NR).transpose(4, 2, 0, 1, 3).reshape(P, NH, NJ, NQ) for s in sides], 1),
        "wout_t": halves(v["out_proj_w"].T),
        "ffn_w": v["L0_ffn_weight"],
        "had": had, "ident_d": ident, "sum_sel_d": sum_sel, "rep_sel_d": rep_sel,
    }
    arrays = {k: np.ascontiguousarray(a) for k, a in arrays.items()}
    nc = bacc.Bacc("TRN2", target_bir_lowering=False, num_devices=1)
    args = [nc.dram_tensor(k, a.shape, F32, kind="ExternalInput").ap() for k, a in arrays.items()]
    out = nc.dram_tensor("out", [NB, L, DM], F32, kind="ExternalOutput").ap()
    build(nc, *args, out)
    r = run_bass_kernel_spmd(nc, [arrays], core_ids=[0])
    return r.results[0]["out"]
```

```python
from contextlib import ExitStack

import numpy as np

import concourse.bass as bass
from concourse import mybir

F32 = mybir.dt.float32
ALU = mybir.AluOpType
ACT = mybir.ActivationFunctionType
AX = mybir.AxisListType

P = 128
NB, L, DM = 8, 512, 128
DI, NS, DR, TAPS = 256, 16, 8, 4
NH = DI // P
CB = 32
NJ = P // CB
NR = P // CB
NQ = NS // NR
SLOTS = NH * NQ
PER_B = 2 * SLOTS
NC = L // P
PAD = TAPS - 1
LN_EPS, Q_FLOOR, Q_POS, Q_NEG = 1e-5, 1e-5, 7.0, 8.0
ROUND = 12582912.0
DMA = 16
XC = 64
REP_DMAS = NJ * NR


def build(nc, x, win_t, wz_t, conv_w, cols, xproj_t, dt_t, a_log, wout_t, ffn_w, had, ident_d, sum_sel_d, rep_sel_d, out):
    ctx = ExitStack()
    with ctx:
        def sb(name, shape):
            return ctx.enter_context(nc.sbuf_tensor(name, shape, F32))

        def sem(name):
            return ctx.enter_context(nc.semaphore(name))

        conv_wt = [sb(f"conv_wt{d}", [P, TAPS, DI]) for d in range(2)]
        wz = sb("wz", [P, DI])
        col = sb("col", [P, 2, 3, NH])
        half_bias = sb("half_bias", [P, 2, NH])
        xproj = [sb(f"xproj{d}", [P, NH, XC]) for d in range(2)]
        dtw = [sb(f"dtw{d}", [P, DI]) for d in range(2)]
        neg_a = sb("neg_a", [P, 2, NH, NJ, NQ])
        skip = sb("skip", [P, 2, NH, P])
        wout = sb("wout", [P, NH, DM])
        wq_t = sb("wq_t", [P, DM])
        fcol = sb("fcol", [P, 4])
        hadm = sb("hadm", [P, DM])
        ident = sb("ident", [P, P])
        sum_sel = sb("sum_sel", [P, CB])
        rep_sel = sb("rep_sel", [P, 2 * NQ, P])
        x_ln = sb("x_ln", [P, NC, DM])
        x_res = sb("x_res", [P, NC, DM])
        stats = sb("stats", [P, NC, 6])
        msum = sb("msum", [P, NC])
        mdiff = sb("mdiff", [P, NC])
        rstd = sb("rstd", [P, NC])
        var = sb("var", [P, NC])
        shift = sb("shift", [P, NC])
        xn = sb("xn", [P, NC, DM])
        xnt = sb("xnt", [P, PAD + L + PAD])
        xnt_kept = sb("xnt_kept", [P, L])
        amax = sb("amax", [P, NC])
        qscale = sb("qscale", [P, NC])
        qinv = sb("qinv", [P, NC])
        xq = sb("xq", [P, NC, DM])
        xqt = sb("xqt", [P, L])
        gate = sb("gate", [P, NH, L])
        y_gated = sb("y_gated", [P, NH, L])
        u = [sb(f"u{d}", [P, NH, L]) for d in range(2)]
        xdbl = [sb(f"xdbl{d}", [P, L]) for d in range(2)]
        t_exp = sb("t_exp", [P, NH, L])
        t_log = sb("t_log", [P, NH, L])
        t_pos = sb("t_pos", [P, NH, L])
        t_cor = sb("t_cor", [P, NH, L])
        dd = [sb(f"dd{h}", [P, 2, L]) for h in range(NH)]
        rep = [[sb(f"rep{d}{h}", [P, 2, NJ, L]) for h in range(NH)] for d in range(2)]
        b_rep = [sb(f"b_rep{d}", [P, NQ, L]) for d in range(2)]
        c_rep = [sb(f"c_rep{d}", [P, NQ, L]) for d in range(2)]
        dbx = [sb(f"dbx{n}", [P, NJ, L]) for n in range(2)]
        hst = [sb(f"hst{n}", [P, NJ, L]) for n in range(2)]
        da = ctx.enter_context(nc.psum_tensor("da", [P, NJ, L], F32))
        y = ctx.enter_context(nc.psum_tensor("y", [P, NH, L], F32))
        pb = ctx.enter_context(nc.psum_tensor("pb", [P, 2, L], F32))

        w_loaded = sem("w_loaded")
        conv_loaded = sem("conv_loaded")
        zeroed = sem("zeroed")
        a_exp = sem("a_exp")
        set_step = sem("set_step")
        fw_ready = sem("fw_ready")
        fwt_filled = sem("fwt_filled")
        fwt_read = sem("fwt_read")
        weights_ready = sem("weights_ready")
        x_loaded = sem("x_loaded")
        xres_loaded = sem("xres_loaded")
        ln_step = sem("ln_step")
        rstd_guess = sem("rstd_guess")
        xn_ready = sem("xn_ready")
        xnt_filled = sem("xnt_filled")
        xnt_ready = sem("xnt_ready")
        kept_ready = sem("kept_ready")
        had_filled = sem("had_filled")
        q_step = sem("q_step")
        had_read = sem("had_read")
        xq_ready = sem("xq_ready")
        xqt_filled = sem("xqt_filled")
        xqt_ready = sem("xqt_ready")
        z_filled = sem("z_filled")
        z_step = sem("z_step")
        z_sig = sem("z_sig")
        gate_ready = sem("gate_ready")
        conv_filled = sem("conv_filled")
        u_step = sem("u_step")
        u_sig = sem("u_sig")
        u_ready = sem("u_ready")
        xdbl_filled = sem("xdbl_filled")
        xdbl_ready = sem("xdbl_ready")
        dt_filled = sem("dt_filled")
        sp_step = sem("sp_step")
        dt_read = sem("dt_read")
        t_ready = sem("t_ready")
        cor_step = sem("cor_step")
        delta_done = sem("delta_done")
        dd_ready = sem("dd_ready")
        rep_loaded = [[sem(f"rep_loaded{d}{h}") for h in range(NH)] for d in range(2)]
        bc_filled = sem("bc_filled")
        bc_ready = sem("bc_ready")
        decay_done = sem("decay_done")
        input_done = sem("input_done")
        scan_done = sem("scan_done")
        prod_done = sem("prod_done")
        sum_done = sem("sum_done")
        y_read = sem("y_read")
        out_filled = sem("out_filled")
        out_ready = sem("out_ready")
        out_stored = sem("out_stored")

        block = ctx.enter_context(nc.Block())

        def wait(eng, s, count):
            if not isinstance(count, int) or count > 0:
                eng.wait_ge(s, count)

        BC = [("b", 0), ("b", 1), ("b", 2), ("c", 0), ("c", 1), ("c", 2), ("b", 3), ("c", 3)]
        BC_BANK = [[1, 0, 1, 0, 1, 0, 1, 0], [1, 0, 1, 0, 0, 1, 1, 0]]
        BC_AT = {bc: n + 1 for n, bc in enumerate(BC)}

        def batches(eng, body):
            body(0)
            with eng.Fori(1, NB - 1) as i:
                body(i)
            body(NB - 1)

        def first(b):
            return isinstance(b, int) and b == 0

        def last(b):
            return isinstance(b, int) and b == NB - 1

        @block.sync
        def _(sp):
            def rows(ap, b):
                return ap[bass.ds(b, 1)].rearrange("b (c p) d -> p (b c) d", p=P)

            def load_x(b):
                src = rows(x, b)
                wait(sp, xn_ready, b)
                sp.dma_start(x_ln[:, :, :], src).then_inc(x_loaded, DMA)

            def load_res(b):
                wait(sp, out_stored, DMA * b)
                sp.dma_start(x_res[:, :, :], rows(x, b)).then_inc(xres_loaded, DMA)

            def store_out(b):
                wait(sp, out_ready, b + 1)
                sp.dma_start(rows(out, b), x_res[:, :, :]).then_inc(out_stored, DMA)

            def spread(d, V):
                for h in range(NH):
                    wait(sp, dd_ready, 2 * V + h + 1)
                    for r in range(NR):
                        for j in range(NJ):
                            sp.dma_start(rep[d][h][CB * r:CB * (r + 1), :, j, :],
                                         dd[h][CB * j:CB * (j + 1), :, :]).then_inc(rep_loaded[d][h], DMA)

            load_x(0)
            for d in range(2):
                sp.dma_start(conv_wt[d][:, :, :], conv_w[d:d + 1].broadcast_to([P, TAPS, DI])).then_inc(conv_loaded, DMA)
            sp.dma_start(wz[:, :], wz_t).then_inc(w_loaded, DMA)
            sp.dma_start(col[:, :, :, :], cols).then_inc(w_loaded, DMA)
            sp.dma_start(neg_a[:, :, :, :, :], a_log).then_inc(w_loaded, DMA)
            sp.dma_start(wout[:, :, :], wout_t).then_inc(w_loaded, DMA)
            sp.dma_start(hadm[:, :], had).then_inc(w_loaded, DMA)
            sp.dma_start(sum_sel[:, :], sum_sel_d).then_inc(w_loaded, DMA)
            sp.dma_start(rep_sel[:, :, :], rep_sel_d).then_inc(w_loaded, DMA)
            sp.wait_ge(zeroed, 4)
            for d in range(2):
                sp.dma_start(xproj[d][:, :, 0:DR + 2 * NS], xproj_t[d]).then_inc(w_loaded, DMA)
                sp.dma_start(dtw[d][0:DR, :], dt_t[d]).then_inc(w_loaded, DMA)
            spread(0, 0)

            def body(b):
                if not last(b):
                    load_x(b + 1)
                spread(1, 2 * b + 1)
                if not first(b):
                    store_out(b - 1)
                load_res(b)
                if not last(b):
                    spread(0, 2 * b + 2)

            batches(sp, body)
            store_out(NB - 1)
            sp.wait_ge(out_stored, DMA * NB)

        W_LOADS = 7 + 4
        WIN = hst[0][:, 0, 0:DI]
        fw = t_cor[:, 0, 0:DM]
        ft = t_cor[:, 0, DM:2 * DM]

        @block.scalar
        def _(act):
            act.dma_start(WIN, win_t).then_inc(conv_loaded, DMA)
            act.dma_start(fw, ffn_w).then_inc(conv_loaded, DMA)
            act.dma_start(ident[:, :], ident_d).then_inc(conv_loaded, DMA)

            def log_var(b):
                act.wait_ge(ln_step, 15 * b + 10)
                nc.scalar.activation(rstd[:, :], var[:, :], ACT.Ln).then_inc(rstd_guess, 1)

            def guess_rstd(b):
                act.wait_ge(rstd_guess, 2 * b + 1)
                nc.scalar.activation(rstd[:, :], rstd[:, :], ACT.Exp, scale=-0.5).then_inc(rstd_guess, 1)

            def normalize(b):
                wait(act, ln_step, 15 * b + 15)
                wait(act, xnt_filled, b)
                for c in range(NC):
                    ins = nc.scalar.activation(xn[:, c, :], x_ln[:, c, :], ACT.Identity, bias=shift[:, c:c + 1], scale=rstd[:, c:c + 1])
                ins.then_inc(xn_ready, 1)

            def keep_xnt(b):
                wait(act, xnt_filled, b + 1)
                wait(act, conv_filled, 4 * b)
                nc.scalar.activation(xnt[:, PAD:PAD + L], pb[:, 1, :], ACT.Copy).then_inc(xnt_ready, 1)

            def keep_longer(b):
                wait(act, xnt_ready, b + 1)
                wait(act, had_filled, b)
                nc.scalar.activation(xnt_kept[:, :], xnt[:, PAD:PAD + L], ACT.Copy).then_inc(kept_ready, 1)

            def keep_xqt(b):
                wait(act, xqt_filled, b + 1)
                wait(act, out_filled, b)
                nc.scalar.activation(xqt[:, :], y[:, 0, :], ACT.Copy).then_inc(xqt_ready, 1)

            def u_tanh(d, V, h):
                wait(act, conv_filled, 2 * V + h + 1)
                wait(act, dd_ready, 2 * V)
                nc.scalar.activation(t_exp[:, h, :], pb[:, h, :], ACT.Tanh, bias=half_bias[:, d, h:h + 1], scale=0.5).then_inc(u_step, 1)

            def u_sigmoid(V):
                act.wait_ge(u_step, 2 * V + 2)
                nc.scalar.activation(t_exp[:, :, :], t_exp[:, :, :], ACT.Copy, bias=0.5, scale=0.5).then_inc(u_sig, 1)

            def z_sigmoid(b):
                wait(act, y_read, 2 * b)
                for h in range(NH):
                    act.wait_ge(z_filled, 2 * b + h + 1)
                    nc.scalar.activation(gate[:, h, :], pb[:, 1 - h, :], ACT.Tanh, scale=0.5).then_inc(z_step, 1)
                act.wait_ge(z_step, 2 * b + 2)
                nc.scalar.activation(gate[:, :, :], gate[:, :, :], ACT.Copy, bias=0.5, scale=0.5).then_inc(z_sig, 1)

            def keep_xdbl(d, V):
                wait(act, xdbl_filled, V + 1)
                wait(act, bc_filled, 8 * V - 8)
                nc.scalar.activation(xdbl[d][0:XC, :], pb[0:XC, 0, :], ACT.Copy).then_inc(xdbl_ready, 1)

            def softplus_exp(d, V):
                wait(act, u_ready, 2 * V + 2)
                for h in range(NH):
                    act.wait_ge(dt_filled, 2 * V + h + 1)
                    nc.scalar.activation(t_exp[:, h, :], pb[:, 1 - h, :], ACT.Abs, bias=col[:, d, 1, h:h + 1]).then_inc(sp_step, 1)
                act.wait_ge(sp_step, 4 * V + 2)
                nc.scalar.activation(t_exp[:, :, :], t_exp[:, :, :], ACT.Exp, scale=-1.0).then_inc(sp_step, 1)

            def softplus_log(d, V):
                wait(act, delta_done, 2 * V)
                act.wait_ge(sp_step, 4 * V + 3)
                nc.scalar.activation(t_cor[:, :, :], t_exp[:, :, :], ACT.Copy, bias=1.0).then_inc(sp_step, 1)
                act.wait_ge(sp_step, 4 * V + 4)
                nc.scalar.activation(t_log[:, :, :], t_cor[:, :, :], ACT.Ln).then_inc(t_ready, 1)
                for h in range(NH):
                    nc.scalar.activation(t_pos[:, h, :], pb[:, 1 - h, :], ACT.Relu, bias=col[:, d, 1, h:h + 1]).then_inc(dt_read, 1)

            def keep_bc(d, V, n):
                kind, q = BC[n]
                act.wait_ge(bc_filled, 8 * V + n + 1)
                if n == 0:
                    wait(act, input_done, SLOTS * (V - 1))
                    wait(act, prod_done, 2 * SLOTS * (V - 1))
                dst = b_rep if kind == "b" else c_rep
                nc.scalar.activation(dst[d][:, q, :], pb[:, BC_BANK[d][n], :], ACT.Copy).then_inc(bc_ready, 1)

            def decays(b, d, s, p):
                S = PER_B * b + SLOTS * d + s
                h, q = divmod(s, NQ)
                if p == 0 and q == 0:
                    wait(act, rep_loaded[d][h], DMA * REP_DMAS * (b + 1))
                wait(act, scan_done, 2 * S + p - 1)
                for j in (2 * p, 2 * p + 1):
                    ins = nc.scalar.activation(da[:, j, 1:L], rep[d][h][:, 0, j, 1:L], ACT.Exp, scale=neg_a[:, d, h, j, q:q + 1])
                ins.then_inc(decay_done, 1)

            act.wait_ge(w_loaded, DMA * W_LOADS)
            nc.scalar.activation(neg_a[:, :, :, :, :], neg_a[:, :, :, :, :], ACT.Exp).then_inc(a_exp, 1)
            log_var(0)
            guess_rstd(0)
            normalize(0)
            keep_xnt(0)
            act.wait_ge(weights_ready, 3)
            u_tanh(0, 0, 0)
            u_tanh(0, 0, 1)
            u_sigmoid(0)
            keep_xdbl(0, 0)
            softplus_exp(0, 0)
            softplus_log(0, 0)
            for n in range(6):
                keep_bc(0, 0, n)

            def unit(b, d):
                U = 2 * b + d
                V, e = U + 1, 1 - d
                nxt = d == 0 or not last(b)
                nb = d == 0 and not last(b)
                for s in range(SLOTS):
                    decays(b, d, s, 0)
                    if s == 0 and d == 0 and not first(b):
                        keep_xqt(b - 1)
                    if s == 4 and nxt:
                        keep_bc(e, V, 0)
                        keep_bc(e, V, 1)
                    if s == 5 and d == 0:
                        keep_longer(b)
                        keep_bc(e, V, 2)
                        keep_bc(e, V, 3)
                    decays(b, d, s, 1)
                    if s == 0 and nxt:
                        u_tanh(e, V, 0)
                        u_tanh(e, V, 1)
                        u_sigmoid(V)
                    if s == 1:
                        if nxt:
                            keep_xdbl(e, V)
                        keep_bc(d, U, 6)
                        keep_bc(d, U, 7)
                    if s == 2 and nxt:
                        softplus_exp(e, V)
                    if s == 3 and nxt:
                        softplus_log(e, V)
                        if nb:
                            log_var(b + 1)
                            guess_rstd(b + 1)
                    if d == 0:
                        if s == 4 and nb:
                            normalize(b + 1)
                        if s == 5:
                            if nb:
                                keep_xnt(b + 1)
                            keep_bc(e, V, 4)
                        if s == 6:
                            keep_bc(e, V, 5)
                    else:
                        if s == 4:
                            z_sigmoid(b)
                        if s in (5, 6) and nxt:
                            keep_bc(e, V, 2 * s - 8)
                            keep_bc(e, V, 2 * s - 7)

            def body(b):
                unit(b, 0)
                unit(b, 1)

            batches(act, body)
            keep_xqt(NB - 1)

        @block.vector
        def _(dve):
            def statistics(b):
                dve.wait_ge(x_loaded, DMA * (b + 1))
                wait(dve, xn_ready, b)
                for c in range(NC):
                    nc.vector.bn_stats(stats[:, c, :], x_ln[:, c, :]).then_inc(ln_step, 1)
                dve.wait_ge(ln_step, 15 * b + 4)
                nc.vector.tensor_tensor(msum[:, :], stats[:, :, 1], stats[:, :, 4], ALU.add).then_inc(ln_step, 1)
                nc.vector.tensor_tensor(mdiff[:, :], stats[:, :, 1], stats[:, :, 4], ALU.subtract).then_inc(ln_step, 1)
                nc.vector.tensor_tensor(var[:, :], stats[:, :, 2], stats[:, :, 5], ALU.add).then_inc(ln_step, 1)
                dve.wait_ge(ln_step, 15 * b + 7)
                nc.vector.scalar_tensor_tensor(mdiff[:, :], mdiff[:, :], 0.25, mdiff[:, :], ALU.mult, ALU.mult).then_inc(ln_step, 1)
                nc.vector.tensor_scalar(var[:, :], var[:, :], 1.0 / DM, LN_EPS, ALU.mult, ALU.add).then_inc(ln_step, 1)
                dve.wait_ge(ln_step, 15 * b + 9)
                nc.vector.tensor_tensor(var[:, :], var[:, :], mdiff[:, :], ALU.add).then_inc(ln_step, 1)

            def refine(b):
                dve.wait_ge(rstd_guess, 2 * b + 2)
                nc.vector.tensor_tensor(shift[:, :], rstd[:, :], rstd[:, :], ALU.mult).then_inc(ln_step, 1)
                dve.wait_ge(ln_step, 15 * b + 11)
                nc.vector.tensor_tensor(shift[:, :], shift[:, :], var[:, :], ALU.mult).then_inc(ln_step, 1)
                dve.wait_ge(ln_step, 15 * b + 12)
                nc.vector.tensor_scalar(shift[:, :], shift[:, :], -0.5, 1.5, ALU.mult, ALU.add).then_inc(ln_step, 1)
                dve.wait_ge(ln_step, 15 * b + 13)
                nc.vector.tensor_tensor(rstd[:, :], rstd[:, :], shift[:, :], ALU.mult).then_inc(ln_step, 1)
                dve.wait_ge(ln_step, 15 * b + 14)
                nc.vector.scalar_tensor_tensor(shift[:, :], msum[:, :], -0.5, rstd[:, :], ALU.mult, ALU.mult).then_inc(ln_step, 1)

            def quantize(b):
                dve.wait_ge(had_filled, b + 1)
                wait(dve, xqt_filled, b)
                xh = y[:, 0, :].rearrange("p (c i) -> p c i", c=NC)
                nc.vector.tensor_reduce(amax[:, :], xh, AX.X, ALU.max, apply_absolute_value=True).then_inc(q_step, 1)
                dve.wait_ge(q_step, 6 * b + 1)
                nc.vector.tensor_scalar(amax[:, :], amax[:, :], Q_FLOOR, None, ALU.max).then_inc(q_step, 1)
                dve.wait_ge(q_step, 6 * b + 2)
                nc.vector.tensor_scalar(qscale[:, :], amax[:, :], 1.0 / Q_POS, None, ALU.mult).then_inc(q_step, 1)
                nc.vector.reciprocal(qinv[:, :], amax[:, :]).then_inc(q_step, 1)
                dve.wait_ge(q_step, 6 * b + 4)
                nc.vector.tensor_scalar(qinv[:, :], qinv[:, :], Q_POS, None, ALU.mult).then_inc(q_step, 1)
                dve.wait_ge(q_step, 6 * b + 5)
                for c in range(NC):
                    ins = nc.vector.tensor_scalar(xq[:, c, :], xh[:, c, :], qinv[:, c:c + 1], ROUND, ALU.mult, ALU.add)
                ins.then_inc(had_read, 1)
                dve.wait_ge(had_read, b + 1)
                nc.vector.tensor_scalar(xq[:, :, :], xq[:, :, :], ROUND, Q_POS, ALU.subtract, ALU.min).then_inc(q_step, 1)
                dve.wait_ge(q_step, 6 * b + 6)
                for c in range(NC):
                    ins = nc.vector.tensor_scalar(xq[:, c, :], xq[:, c, :], -Q_NEG, qscale[:, c:c + 1], ALU.max, ALU.mult)
                ins.then_inc(xq_ready, 1)

            def gates(b):
                dve.wait_ge(z_sig, b + 1)
                for h in range(NH):
                    nc.vector.tensor_tensor(gate[:, h, :], pb[:, 1 - h, :], gate[:, h, :], ALU.mult).then_inc(gate_ready, 1)

            def make_u(d, V):
                dve.wait_ge(u_sig, V + 1)
                wait(dve, sum_done, SLOTS * (V - 1))
                for h in range(NH):
                    nc.vector.scalar_tensor_tensor(u[d][:, h, :], pb[:, h, :], col[:, d, 0, h:h + 1], t_exp[:, h, :], ALU.add, ALU.mult).then_inc(u_ready, 1)

            def log1p(V):
                dve.wait_ge(t_ready, V + 1)
                nc.vector.scalar_tensor_tensor(t_cor[:, :, :], t_cor[:, :, :], 1.0, t_log[:, :, :], ALU.subtract, ALU.subtract).then_inc(cor_step, 1)
                dve.wait_ge(cor_step, 2 * V + 1)
                nc.vector.scalar_tensor_tensor(t_cor[:, :, :], t_cor[:, :, :], 0.0, t_exp[:, :, :], ALU.max, ALU.subtract).then_inc(cor_step, 1)

            def scan_input(b, d, s):
                S = PER_B * b + SLOTS * d + s
                h, q = divmod(s, NQ)
                dve.wait_ge(bc_ready, 8 * (2 * b + d) + BC_AT["b", q])
                if q == 0:
                    dve.wait_ge(rep_loaded[d][h], DMA * REP_DMAS * (b + 1))
                wait(dve, scan_done, 2 * (S - 1))
                nc.vector.tensor_tensor(dbx[s % 2][:, :, :], rep[d][h][:, 1, :, :], b_rep[d][:, q:q + 1, :].broadcast_to([P, NJ, L]), ALU.mult).then_inc(input_done, 1)

            def scan(b, d, s, p):
                S = PER_B * b + SLOTS * d + s
                dve.wait_ge(decay_done, 2 * S + p + 1)
                if p == 0:
                    dve.wait_ge(input_done, S + 1)
                    wait(dve, sum_done, S - 1)
                two = slice(2 * p, 2 * p + 2)
                nc.vector.tensor_tensor_scan(hst[s % 2][:, two, :].rearrange("p j l -> p (j l)"),
                                             da[:, two, :].rearrange("p j l -> p (j l)"),
                                             dbx[s % 2][:, two, :].rearrange("p j l -> p (j l)"),
                                             0.0, ALU.mult, ALU.add).then_inc(scan_done, 1)

            def gate_y(b, h):
                dve.wait_ge(sum_done, PER_B * b + SLOTS + NQ * (h + 1))
                dve.wait_ge(gate_ready, 2 * b + 2)
                wait(dve, out_filled, b)
                nc.vector.tensor_tensor(y_gated[:, h, :], y[:, h, :], gate[:, h, :], ALU.mult).then_inc(y_read, 1)

            def add_residual(b):
                dve.wait_ge(out_filled, b + 1)
                dve.wait_ge(xres_loaded, DMA * (b + 1))
                nc.vector.tensor_tensor(x_res[:, :, :], y[:, 1, :].rearrange("p (c o) -> p c o", c=NC), x_res[:, :, :], ALU.add).then_inc(out_ready, 1)

            for d in range(2):
                nc.vector.memset(xproj[d][:, :, :], 0.0).then_inc(zeroed, 1)
                nc.vector.memset(dtw[d][:, :], 0.0).then_inc(zeroed, 1)
            for d in range(2):
                nc.vector.memset(xnt[:, d * (PAD + L):d * (PAD + L) + PAD], 0.0)
                nc.vector.memset(xdbl[d][XC:P, :], 0.0)
            nc.vector.memset(da[:, :, 0:1], 0.0).then_inc(zeroed, 1)
            statistics(0)
            refine(0)
            dve.wait_ge(conv_loaded, DMA * 5)
            for d in range(2):
                nc.vector.tensor_tensor(conv_wt[d][:, :, :], conv_wt[d][:, :, :], hst[0][:, 0:1, 0:DI].broadcast_to([P, TAPS, DI]), ALU.mult).then_inc(weights_ready, 1)
            dve.wait_ge(w_loaded, DMA * W_LOADS)
            nc.vector.tensor_scalar(half_bias[:, :, :], col[:, :, 0, :], 0.5, None, ALU.mult).then_inc(weights_ready, 1)
            for d in range(2):
                for h in range(NH):
                    nc.vector.tensor_scalar(skip[:, d, h, :], ident[:, :], col[:, d, 2, h:h + 1], None, ALU.mult).then_inc(set_step, 1)
            dve.wait_ge(a_exp, 1)
            nc.vector.tensor_scalar(neg_a[:, :, :, :, :], neg_a[:, :, :, :, :], -1.0, None, ALU.mult).then_inc(weights_ready, 1)
            nc.vector.tensor_reduce(fcol[:, 0:1], fw, AX.X, ALU.add, apply_absolute_value=True).then_inc(set_step, 1)
            dve.wait_ge(set_step, 5)
            nc.vector.tensor_scalar(fcol[:, 1:2], fcol[:, 0:1], 1.0 / DM, Q_FLOOR, ALU.mult, ALU.max).then_inc(set_step, 1)
            dve.wait_ge(set_step, 6)
            nc.vector.tensor_scalar(fcol[:, 2:3], fcol[:, 1:2], 0.5, None, ALU.mult).then_inc(set_step, 1)
            nc.vector.tensor_scalar(fcol[:, 3:4], fcol[:, 1:2], -0.5, None, ALU.mult).then_inc(set_step, 1)
            dve.wait_ge(set_step, 8)
            nc.vector.tensor_scalar(ft, fw, fcol[:, 3:4], None, ALU.is_lt).then_inc(set_step, 1)
            dve.wait_ge(set_step, 9)
            nc.vector.scalar_tensor_tensor(ft, fw, fcol[:, 2:3], ft, ALU.is_gt, ALU.subtract).then_inc(set_step, 1)
            dve.wait_ge(set_step, 10)
            nc.vector.tensor_scalar(ft, ft, fcol[:, 1:2], None, ALU.mult).then_inc(fw_ready, 1)
            dve.wait_ge(fwt_filled, 1)
            nc.vector.tensor_copy(wq_t[:, :], pb[:, 0, 0:DM]).then_inc(fwt_read, 1)
            make_u(0, 0)
            log1p(0)
            scan_input(0, 0, 0)

            def unit(b, d):
                U = 2 * b + d
                V, e = U + 1, 1 - d
                nxt = d == 0 or not last(b)
                for s in range(SLOTS):
                    if s < SLOTS - 1:
                        scan_input(b, d, s + 1)
                    elif nxt:
                        scan_input(b + d, e, 0)
                    if s == 5 and d == 1:
                        gates(b)
                    scan(b, d, s, 0)
                    if s == 4 and d == 0 and not last(b):
                        refine(b + 1)
                    scan(b, d, s, 1)
                    if s == 0 and nxt:
                        make_u(e, V)
                    if s == 3 and nxt:
                        log1p(V)
                    if d == 0:
                        if s == 1 and not first(b):
                            gate_y(b - 1, 1)
                        if s == 2 and not last(b):
                            statistics(b + 1)
                        if s == 4 and not first(b):
                            add_residual(b - 1)
                    else:
                        if s == 5:
                            gate_y(b, 0)
                        if s == 6:
                            quantize(b)

            def body(b):
                unit(b, 0)
                unit(b, 1)

            batches(dve, body)
            gate_y(NB - 1, 1)
            add_residual(NB - 1)

        @block.gpsimd
        def _(pool):
            def states_times_c(b, d, s, p):
                S = PER_B * b + SLOTS * d + s
                q = s % NQ
                pool.wait_ge(scan_done, 2 * S + p + 1)
                if p == 0:
                    pool.wait_ge(bc_ready, 8 * (2 * b + d) + BC_AT["c", q])
                two = slice(2 * p, 2 * p + 2)
                nc.gpsimd.tensor_tensor(hst[s % 2][:, two, :], hst[s % 2][:, two, :], c_rep[d][:, q:q + 1, :].broadcast_to([P, 2, L]), ALU.mult).then_inc(prod_done, 1)

            def delta(d, V, b, h):
                pool.wait_ge(cor_step, 2 * V + 2)
                pool.wait_ge(dt_read, 2 * V + 2)
                pool.wait_ge(u_ready, 2 * V + 2)
                wait(pool, rep_loaded[1 - d][h], DMA * REP_DMAS * (b + d))
                nc.gpsimd.tensor_tensor(dd[h][:, 0, :], t_pos[:, h, :], t_cor[:, h, :], ALU.subtract).then_inc(delta_done, 1)
                pool.wait_ge(delta_done, 2 * V + h + 1)
                nc.gpsimd.tensor_tensor(dd[h][:, 1, :], dd[h][:, 0, :], u[d][:, h, :], ALU.mult).then_inc(dd_ready, 1)

            delta(0, 0, 0, 0)
            delta(0, 0, 0, 1)

            def unit(b, d):
                for s in range(SLOTS):
                    states_times_c(b, d, s, 0)
                    states_times_c(b, d, s, 1)
                    if s in (3, 4) and (d == 0 or not last(b)):
                        delta(1 - d, 2 * b + d + 1, b + d, s - 3)

            def body(b):
                unit(b, 0)
                unit(b, 1)

            batches(pool, body)

        @block.tensor
        def _(pe):
            mm = nc.tensor.matmul

            def conv(d, V, h, free, count):
                wait(pe, free, count)
                for k in range(TAPS):
                    end = 2 * PAD + L - k
                    window = xnt[:, end - 1:end - 1 - L:-1] if d else xnt[:, k:k + L]
                    ins = mm(pb[:, h, :], conv_wt[d][:, k, P * h:P * (h + 1)], window, start=k == 0, stop=k == TAPS - 1)
                ins.then_inc(conv_filled, 1)

            def x_proj(d, V):
                pe.wait_ge(u_ready, 2 * V + 2)
                for h in range(NH):
                    ins = mm(pb[0:XC, 0, :], xproj[d][:, h, :], u[d][:, h, :], start=h == 0, stop=h == NH - 1)
                ins.then_inc(xdbl_filled, 1)

            def steps(d, V, free, counts):
                pe.wait_ge(xdbl_ready, V + 1)
                for h in range(NH):
                    wait(pe, free, counts[h])
                    mm(pb[:, 1 - h, :], dtw[d][:, P * h:P * (h + 1)], xdbl[d][:, :], start=True, stop=True).then_inc(dt_filled, 1)

            def spread_bc(d, V, n, free, count):
                kind, q = BC[n]
                wait(pe, free, count)
                mm(pb[:, BC_BANK[d][n], :], rep_sel[:, q + NQ * (kind == "c"), :], xdbl[d][:, :], start=True, stop=True).then_inc(bc_filled, 1)

            def transpose_xn(b, free, count):
                wait(pe, xn_ready, b + 1)
                wait(pe, free, count)
                for c in range(NC):
                    ins = nc.tensor.transpose(pb[:, 1, P * c:P * (c + 1)], xn[:, c, :], ident[:, :])
                ins.then_inc(xnt_filled, 1)

            def hadamard(b):
                wait(pe, y_read, 2 * b + 1)
                for c in range(NC):
                    ins = mm(y[:, 0, P * c:P * (c + 1)], xnt_kept[:, P * c:P * (c + 1)], hadm[:, :], start=True, stop=True)
                ins.then_inc(had_filled, 1)

            def transpose_xq(b):
                pe.wait_ge(xq_ready, b + 1)
                for c in range(NC):
                    ins = nc.tensor.transpose(y[:, 0, P * c:P * (c + 1)], xq[:, c, :], ident[:, :])
                ins.then_inc(xqt_filled, 1)

            def z_proj(b, h, free, count):
                wait(pe, kept_ready, b + 1)
                wait(pe, free, count)
                mm(pb[:, 1 - h, :], wz[:, P * h:P * (h + 1)], xnt_kept[:, :], start=True, stop=True).then_inc(z_filled, 1)

            def sum_states(b, d, s):
                S = PER_B * b + SLOTS * d + s
                h, q = divmod(s, NQ)
                step = slice(None, None, -1 if d else 1)
                if q == 0:
                    if d == 0:
                        wait(pe, out_ready if h else xqt_ready, b)
                    pe.wait_ge(u_ready, 2 * (2 * b + d) + 2)
                    mm(y[:, h, :], skip[:, d, h, :], u[d][:, h, step], start=d == 0, stop=False, skip_group_check=True)
                pe.wait_ge(prod_done, 2 * S + 2)
                for j in range(NJ):
                    ins = mm(y[CB * j:CB * (j + 1), h, :], sum_sel[:, :], hst[s % 2][:, j, step],
                             start=False, stop=d == 1 and q == NQ - 1, skip_group_check=True)
                ins.then_inc(sum_done, 1)

            def project(b):
                pe.wait_ge(y_read, 2 * b + 2)
                pe.wait_ge(xqt_ready, b + 1)
                for c in range(NC):
                    at = slice(P * c, P * (c + 1))
                    mm(y[:, 1, at], xqt[:, at], wq_t[:, :], start=True, stop=False)
                    for h in range(NH):
                        ins = mm(y[:, 1, at], y_gated[:, h, at], wout[:, h, :], start=False, stop=h == NH - 1)
                ins.then_inc(out_filled, 1)

            pe.wait_ge(conv_loaded, DMA * 5)
            pe.wait_ge(zeroed, 5)
            transpose_xn(0, xn_ready, 1)
            pe.wait_ge(fw_ready, 1)
            nc.tensor.transpose(pb[:, 0, 0:DM], ft, ident[:, :]).then_inc(fwt_filled, 1)
            pe.wait_ge(w_loaded, DMA * W_LOADS)
            pe.wait_ge(weights_ready, 4)
            pe.wait_ge(xnt_ready, 1)
            conv(0, 0, 0, fwt_read, 1)
            conv(0, 0, 1, xnt_ready, 1)
            x_proj(0, 0)
            steps(0, 0, xdbl_ready, (1, 1))
            for n, (free, count) in enumerate([(dt_read, 1), (dt_read, 2)] + [(bc_ready, m) for m in (1, 2, 3, 4)]):
                spread_bc(0, 0, n, free, count)
            conv(1, 1, 0, bc_ready, 6)
            conv(1, 1, 1, bc_ready, 6)

            def unit(b, d):
                U = 2 * b + d
                V, e = U + 1, 1 - d
                nxt = d == 0 or not last(b)
                for s in range(SLOTS):
                    if s == 1:
                        if nxt:
                            x_proj(e, V)
                            spread_bc(d, U, 6, u_ready, 2 * V + 2)
                            spread_bc(d, U, 7, xdbl_ready, V + 1)
                        else:
                            spread_bc(d, U, 6, bc_ready, 8 * U + 6)
                            spread_bc(d, U, 7, bc_ready, 8 * U + 6)
                    if s == 2 and nxt:
                        steps(e, V, bc_ready, (8 * U + 7, 8 * U + 8))
                    if d == 0:
                        if s == 0 and not first(b):
                            transpose_xq(b - 1)
                        if s == 4:
                            spread_bc(e, V, 2, bc_ready, 8 * V + 1)
                            spread_bc(e, V, 3, bc_ready, 8 * V + 2)
                        if s == 5:
                            if not last(b):
                                transpose_xn(b + 1, bc_ready, 8 * V + 3)
                            spread_bc(e, V, 4, bc_ready, 8 * V + 4)
                        if s == 6:
                            if last(b):
                                spread_bc(e, V, 5, bc_ready, 8 * V + 3)
                            else:
                                spread_bc(e, V, 5, xnt_ready, b + 2)
                                conv(0, V + 1, 0, bc_ready, 8 * V + 5)
                        if s == 7 and not last(b):
                            conv(0, V + 1, 1, bc_ready, 8 * V + 6)
                    else:
                        if s == 4:
                            z_proj(b, 0, bc_ready, 8 * V + 1 if nxt else 8 * U + 7)
                            z_proj(b, 1, bc_ready, 8 * V + 2 if nxt else 8 * U + 8)
                        if s == 5 and nxt:
                            spread_bc(e, V, 2, gate_ready, 2 * b + 1)
                            spread_bc(e, V, 3, gate_ready, 2 * b + 2)
                        if s == 6:
                            hadamard(b)
                            if nxt:
                                spread_bc(e, V, 4, bc_ready, 8 * V + 3)
                                spread_bc(e, V, 5, bc_ready, 8 * V + 4)
                        if s == 7 and nxt:
                            conv(1, V + 1, 0, bc_ready, 8 * V + 6)
                            conv(1, V + 1, 1, bc_ready, 8 * V + 6)
                    if s > 0:
                        sum_states(b, d, s - 1)
                    elif d == 1:
                        sum_states(b, 0, SLOTS - 1)
                    elif not first(b):
                        sum_states(b - 1, 1, SLOTS - 1)
                    if d == 0 and s == 2 and not first(b):
                        project(b - 1)
                    if s == 3 and nxt:
                        spread_bc(e, V, 0, dt_read, 2 * V + 1)
                        spread_bc(e, V, 1, dt_read, 2 * V + 2)

            def body(b):
                unit(b, 0)
                unit(b, 1)

            batches(pe, body)
            transpose_xq(NB - 1)
            sum_states(NB - 1, 1, SLOTS - 1)
            project(NB - 1)


def constants():
    had = np.array([[1.0]])
    while had.shape[0] < DM:
        had = np.block([[had, had], [had, -had]])
    had = (had / np.sqrt(DM)).astype(np.float32)
    ident = np.eye(P, dtype=np.float32)
    sum_sel = np.tile(np.eye(CB, dtype=np.float32), (NR, 1))
    rep_sel = np.zeros((P, 2 * NQ, P), np.float32)
    for g in range(2 * NQ):
        for r in range(NR):
            rep_sel[DR + NR * g + r, g, CB * r:CB * (r + 1)] = 1.0
    return had, ident, sum_sel, rep_sel


def kernel(**inputs):
    import concourse.bacc as bacc
    from concourse.bass_utils import run_bass_kernel_spmd

    v = {k.replace("L0_attn_", ""): np.asarray(a) for k, a in inputs.items()}
    sides = [("conv_w", "conv_bias", "x_proj_w", "dt_proj_w", "dt_proj_bias", "A_log", "D_skip"),
             ("convb_w", "convb_bias", "x_proj_b_w", "dt_proj_b_w", "dt_proj_b_bias", "A_b_log", "D_b_skip")]

    def halves(a):
        return np.moveaxis(a.reshape(NH, P, *a.shape[1:]), 0, 1)

    had, ident, sum_sel, rep_sel = constants()
    arrays = {
        "x": v["hidden_states"],
        "win_t": v["in_proj_w"][:DI].T,
        "wz_t": v["in_proj_w"][DI:].T,
        "conv_w": np.stack([v[s[0]][:, 0, :].T for s in sides]),
        "cols": np.stack([np.stack([halves(v[s[n]]) for n in (1, 4, 6)], 1) for s in sides], 1),
        "xproj_t": np.stack([halves(v[s[2]].T) for s in sides]),
        "dt_t": np.stack([v[s[3]].T for s in sides]),
        "a_log": np.stack([v[s[5]].reshape(NH, NJ, CB, NQ, NR).transpose(4, 2, 0, 1, 3).reshape(P, NH, NJ, NQ) for s in sides], 1),
        "wout_t": halves(v["out_proj_w"].T),
        "ffn_w": v["L0_ffn_weight"],
        "had": had, "ident_d": ident, "sum_sel_d": sum_sel, "rep_sel_d": rep_sel,
    }
    arrays = {k: np.ascontiguousarray(a) for k, a in arrays.items()}
    nc = bacc.Bacc("TRN2", target_bir_lowering=False, num_devices=1)
    args = [nc.dram_tensor(k, a.shape, F32, kind="ExternalInput").ap() for k, a in arrays.items()]
    out = nc.dram_tensor("out", [NB, L, DM], F32, kind="ExternalOutput").ap()
    build(nc, *args, out)
    r = run_bass_kernel_spmd(nc, [arrays], core_ids=[0])
    return r.results[0]["out"]
```
